# Optimizing a Trainium2 kernel written in Bass

```python
import numpy as np
import jax
import jax.numpy as jnp

def _softmax(x, axis=-1):
    return jax.nn.softmax(x, axis=axis)

def _gelu(x):
    return jax.nn.gelu(x, approximate=True)

def _silu(x):
    return jax.nn.silu(x)

def _sigmoid(x):
    return jax.nn.sigmoid(x)

def _layernorm(x, axis=-1, eps=1e-05):
    m = jnp.mean(x, axis=axis, keepdims=True)
    v = jnp.var(x, axis=axis, keepdims=True)
    return (x - m) / jnp.sqrt(v + eps)

def _scatter_add(tgt, idx, src, axis=0):
    return tgt.at[idx].add(src)

def _segment_sum(src, seg, n):
    return jax.ops.segment_sum(src, seg, n)
kernel_name = 'mk_adj_resnorm_d1_adj_r2_46f6d3'

def setup_inputs(seed: int=0):
    np.random.seed(seed)
    _w = jnp.asarray

    def _rec_inputs():
        import jax
        import jax.numpy as jnp
        _gk = jax.random.key(seed)
        x = -0.000929 + 1 * jax.random.normal(jax.random.fold_in(_gk, 1), (8192, 128), jnp.float32)
        _a = jax.random.bernoulli(jax.random.fold_in(_gk, 2), 0.000488281, (8192, 8192))
        _a = jnp.logical_or(_a, jnp.swapaxes(_a, -1, -2))
        _a = jnp.logical_or(_a, jnp.eye(8192, dtype=bool))
        _af = _a.astype(jnp.float32)
        _af = _af * jax.random.uniform(jax.random.fold_in(_gk, 3), (8192, 8192), jnp.float32, 0.05, 1)
        adj = _af
        return (x, adj)
    x, adj = _rec_inputs()

    def _L0_gnn_setup():
        import jax, jax.numpy as jnp
        import numpy as np
        N, IN_F, OUT_F = (4096, 128, 128)
        key = jax.random.key(seed)
        k1, k2, k3 = jax.random.split(key, 3)
        x = jax.random.normal(k1, (N, IN_F), dtype=jnp.float32)
        adj = jax.random.uniform(k2, (N, N), dtype=jnp.float32)
        limit = np.sqrt(6.0 / (IN_F + OUT_F)).astype(np.float32)
        weight = jax.random.uniform(k3, (IN_F, OUT_F), dtype=jnp.float32, minval=-limit, maxval=limit)
        return {'x': x, 'adj': adj, 'weight': weight}
    _L0_gnn_all = _L0_gnn_setup()
    _L0_gnn_in = {k: v for k, v in _L0_gnn_all.items() if k in ('weight',)}
    del _L0_gnn_all
    return {'x': x, 'adj': adj, 'L0_gnn_weight': _L0_gnn_in['weight']}

def reference(x, adj, L0_gnn_weight):
    import jax
    import jax.numpy as jnp

    def _L0_gnn_ref(x, adj, weight):
        import jax, jax.numpy as jnp
        import numpy as np
        N, IN_F, OUT_F = (4096, 128, 128)
        degree = jnp.sum(adj, axis=1)
        d_is = degree ** (-0.5)
        normalized_adj = d_is[:, None] * adj * d_is[None, :]
        support = x @ weight
        out = normalized_adj @ support
        return out
    x = _layernorm(x + _L0_gnn_ref(x, adj, L0_gnn_weight), axis=-1)
    return x

_drawn_inputs = setup_inputs


def setup_inputs(seed=0):
    import zlib

    import numpy as np

    out = dict(_drawn_inputs(seed))
    spreads = {}
    factors = {}
    for name, (base, spread) in spreads.items():
        noise = np.random.default_rng([zlib.crc32(name.encode()), seed]).standard_normal(out[name].shape)
        drawn = base * np.exp(spread * noise) if base else spread * noise
        out[name] = jnp.asarray(drawn.astype(out[name].dtype))
    for name, factor in factors.items():
        out[name] = (out[name] * factor).astype(out[name].dtype)
    return out
```

```python
from contextlib import ExitStack

import concourse.bass as bass
from concourse import mybir

F32 = mybir.dt.float32
ALU = mybir.AluOpType
ACT = mybir.ActivationFunctionType
AX_X = mybir.AxisListType.X

P = 128
N = 8192
F = 128
B = 4
C = B * P
S = N // C
NEAR = 3
RING = 4
BANKS = 4
FAR_RING = 6
EPS = 1e-5
TAIL = 2

CACHE_AT = [d * (d + 1) // 2 for d in range(NEAR + 1)]
CACHE_SLOTS = CACHE_AT[NEAR] + NEAR + 1


def cached_count(k):
    return 1 + min(NEAR, k)


def stream_count(k):
    return S - cached_count(k)


def stream_before(k):
    return sum(stream_count(t) for t in range(k))


def far_count(r):
    return max(0, S - 1 - NEAR - r)


def kept_count(r):
    return min(NEAR, S - 1 - r) + 1


def load_order(k):
    kept = [("kept", d) for d in range(kept_count(k + 1))] if k + 1 < S else []
    far = [("far", n) for n in range(far_count(k + 1))] if k + 1 < S else []
    if k < 0:
        out = []
        while kept or far:
            out += kept[:1] + far[:3]
            kept, far = kept[1:], far[3:]
        return out
    streams = [("stream", m) for m in range(stream_count(k))]
    head = cached_count(k) + 1
    extras = far[:head] + kept + far[head:]
    out, room, extras = streams[:RING] + extras[:head], streams[RING:-TAIL], extras[head:]
    for i, s in enumerate(room):
        out += extras[len(extras) * i // len(room):len(extras) * (i + 1) // len(room)]
        out.append(s)
    return out + streams[-TAIL:]


def gnn_layernorm(nc, adj_t, adj_n, x_t, x_n, weight, out):
    with ExitStack() as ctx:
        def sb(name, shape):
            return ctx.enter_context(nc.sbuf_tensor(name, shape, F32))

        def psum(name, shape):
            return ctx.enter_context(nc.psum_tensor(name, shape, F32))

        def sem(name):
            return ctx.enter_context(nc.semaphore(name))

        stream = sb("stream", [P, RING, B, C])
        cache = sb("cache", [P, CACHE_SLOTS * B * C])
        natural = sb("natural", [P, FAR_RING, C])
        row_acc = sb("row_acc", [P, S, C])
        out_acc = sb("out_acc", [P, N])
        pair_sum = sb("pair_sum", [P, 2, C])
        quad_sum = sb("quad_sum", [P, 2, C])
        row_parts = sb("row_parts", [P, C])
        scaled = sb("scaled", [P, 2, B, F])
        xt = sb("xt", [P, C])
        w_sb = sb("w_sb", [P, F])
        ident = sb("ident", [P, P])
        ones = sb("ones", [P, 1])
        minus_half = sb("minus_half", [P, B])
        far_parts = sb("far_parts", [P, B, S])
        far_sum = sb("far_sum", [P, B])
        degree = sb("degree", [P, B])
        d_is = sb("d_is", [P, S, B])
        stats = sb("stats", [P, 2, B, 6])
        mean_var = sb("mean_var", [P, 2, B, 2])
        var_eps = sb("var_eps", [P, 2, B])
        rstd = sb("rstd", [P, 2, B])
        shift = sb("shift", [P, 2, B])
        stage = row_acc[:, 0:2, :]
        y = row_acc[:, 2:4, :].rearrange("p a (b f) -> p a b f", b=B)
        result = row_acc[:, 4:6, :].rearrange("p a (b f) -> p a b f", b=B)
        x_res = row_acc[:, 6:10, :].rearrange("p a (b f) -> p a b f", b=B)
        XR = 4

        prod = psum("prod", [P, BANKS, C])
        support = psum("support", [P, B, F])
        deg_ps = psum("deg_ps", [P, C])
        turned = psum("turned", [P, 2, B, F])

        stream_loaded = [sem(f"stream_loaded{i}") for i in range(RING)]
        kept_loaded = [sem(f"kept_loaded{i}") for i in range(NEAR + 1)]
        natural_loaded = [sem(f"natural_loaded{i}") for i in range(FAR_RING)]
        weight_loaded = sem("weight_loaded")
        xt_loaded = sem("xt_loaded")
        xres_loaded = [sem(f"xres_loaded{i}") for i in range(XR)]
        consts_ready = sem("consts_ready")
        ident_zero = sem("ident_zero")
        chunk_multiplied = sem("chunk_multiplied")
        chunk_folded = sem("chunk_folded")
        pair_done = sem("pair_done")
        quad_done = sem("quad_done")
        row_added = sem("row_added")
        natural_summed = sem("natural_summed")
        far_reduced = sem("far_reduced")
        row_parts_ready = sem("row_parts_ready")
        support_ready = sem("support_ready")
        degree_parts_ready = sem("degree_parts_ready")
        degree_ready = sem("degree_ready")
        d_is_ready = sem("d_is_ready")
        scaled_ready = sem("scaled_ready")
        turned_ready = sem("turned_ready")
        y_ready = sem("y_ready")
        stats_ready = sem("stats_ready")
        mean_ready = sem("mean_ready")
        var_ready = sem("var_ready")
        rstd_ready = sem("rstd_ready")
        shift_ready = sem("shift_ready")
        result_ready = sem("result_ready")
        stored = [sem(f"stored{i}") for i in range(2)]

        def chunk_of(k, pos):
            n = cached_count(k)
            return k - pos if pos < n else (k + 1 + pos - n) % S

        summed = {}
        for k in range(-1, S):
            for kind, m in load_order(k):
                if kind == "stream" and k + 1 + m < S:
                    summed["stream", k, m] = len(summed)
                if kind == "kept":
                    summed["kept", k + 1, m] = len(summed)

        block = ctx.enter_context(nc.Block())

        @block.sync
        def _(sp):
            sp.dma_start(w_sb[:, :], weight).then_inc(weight_loaded, 16)

            def load_xt(r):
                if r > 0:
                    sp.wait_ge(support_ready, r)
                sp.dma_start(xt[:, :], x_t[r]).then_inc(xt_loaded, 16)

            def load_x_res(p):
                if p >= XR:
                    sp.wait_ge(y_ready, B * (p - XR + 1))
                sp.dma_start(x_res[:, p % XR, :, :], x_n[chunk_of(S - 1, p)])\
                    .then_inc(xres_loaded[p % XR], 16)

            far_seen = 0
            load_xt(0)
            for k in range(-1, S):
                if k >= 0 and k + 1 < S:
                    load_xt(k + 1)
                if k == S - 1:
                    sp.wait_ge(row_parts_ready, S)
                    for p in range(cached_count(k)):
                        load_x_res(p)
                for kind, m in load_order(k):
                    if k == S - 1:
                        load_x_res(cached_count(k) + m)
                    if kind == "stream":
                        q = stream_before(k) + m
                        if q >= RING:
                            kk, mm = k, m - RING
                            while mm < 0:
                                kk -= 1
                                mm += stream_count(kk)
                            sp.wait_ge(chunk_multiplied, S * kk + cached_count(kk) + mm + 1)
                            if ("stream", kk, mm) in summed:
                                sp.wait_ge(pair_done, summed["stream", kk, mm] + 1)
                        sp.dma_start(stream[:, q % RING, :, :], adj_t[k, (k + 1 + m) % S])\
                            .then_inc(stream_loaded[q % RING], 16)
                    if kind == "kept":
                        r, d = k + 1, m
                        if r - d - 1 >= 0:
                            sp.wait_ge(chunk_multiplied, S * k + d + 1)
                        if r > 0:
                            sp.wait_ge(kept_loaded[d], 16 * r)
                        at = (CACHE_AT[d] + r % (d + 1)) * B * C
                        sp.dma_start(cache[:, at:at + B * C],
                                     adj_t[r + d, r].rearrange("p b c -> p (b c)"))\
                            .then_inc(kept_loaded[d], 16)
                    if kind == "far":
                        r, n = k + 1, m
                        for b in range(B):
                            z = B * far_seen + b
                            if z >= FAR_RING:
                                sp.wait_ge(natural_summed, z - FAR_RING + 1)
                            sp.dma_start(natural[:, z % FAR_RING, :],
                                         adj_n[r, r + NEAR + 1 + n, b])\
                                .then_inc(natural_loaded[z % FAR_RING], 16)
                        far_seen += 1

        @block.gpsimd
        def _(pool):
            nc.gpsimd.memset(ident[:, :], 0.0).then_inc(ident_zero, 1)
            nc.gpsimd.memset(ones[:, :], 1.0).then_inc(consts_ready, 1)
            nc.gpsimd.memset(minus_half[:, :], -0.5).then_inc(consts_ready, 1)
            pool.wait_ge(ident_zero, 1)
            nc.gpsimd.affine_select(out=ident[:, :], in_=ident[:, :], compare_op=ALU.not_equal,
                                    fill=1.0, base=0, pattern=[[-1, P]], channel_multiplier=1)\
                .then_inc(consts_ready, 1)
            pool.wait_ge(consts_ready, 3)
            for r in range(S):
                pool.wait_ge(degree_ready, r + 1)
                nc.gpsimd.tensor_tensor(d_is[:, r, :], degree[:, :], minus_half[:, :], ALU.pow)\
                    .then_inc(d_is_ready, 1)
            for p in range(S):
                pool.wait_ge(var_ready, p + 1)
                if p >= 2:
                    pool.wait_ge(result_ready, B * (p - 1))
                nc.gpsimd.tensor_tensor(rstd[:, p % 2, :], var_eps[:, p % 2, :], minus_half[:, :],
                                        ALU.pow).then_inc(rstd_ready, 1)

        @block.scalar
        def _(act):
            far_seen = 0
            for r in range(S):
                if far_count(r) and r > 0:
                    act.wait_ge(far_reduced, r)
                for n in range(far_count(r)):
                    for b in range(B):
                        z = B * far_seen + b
                        act.wait_ge(natural_loaded[z % FAR_RING], 16 * (z // FAR_RING + 1))
                        block_in = natural[:, z % FAR_RING, :]
                        nc.scalar.activation(block_in, block_in, ACT.Copy,
                                             accum_out=far_parts[:, b, n:n + 1])\
                            .then_inc(natural_summed, 1)
                    far_seen += 1
                act.wait_ge(support_ready, r + 1)
                act.wait_ge(d_is_ready, r + 1)
                if r >= 2:
                    act.wait_ge(chunk_multiplied, S * (r - 1))
                for b in range(B):
                    nc.scalar.activation(scaled[:, r % 2, b, :], support[:, b, :], ACT.Copy,
                                         scale=d_is[:, r, b:b + 1]).then_inc(scaled_ready, 1)
            for p in range(S):
                act.wait_ge(shift_ready, p + 1)
                if p >= 2:
                    act.wait_ge(stored[p % 2], 16 * (p // 2))
                for b in range(B):
                    nc.scalar.activation(result[:, p % 2, b, :], y[:, p % 2, b, :], ACT.Identity,
                                         scale=rstd[:, p % 2, b:b + 1],
                                         bias=shift[:, p % 2, b:b + 1]).then_inc(result_ready, 1)
                act.wait_ge(result_ready, B * (p + 1))
                act.dma_start(out[chunk_of(S - 1, p)], result[:, p % 2, :, :])\
                    .then_inc(stored[p % 2], 16)
            for i in range(2):
                act.wait_ge(stored[i], 16 * (S // 2))

        @block.tensor
        def _(pe):
            def prepare(r, first=False):
                pe.wait_ge(xt_loaded, 16 * (r + 1))
                if first:
                    pe.wait_ge(weight_loaded, 16)
                    pe.wait_ge(consts_ready, 3)
                else:
                    pe.wait_ge(scaled_ready, B * r)
                for b in range(B):
                    ins = nc.tensor.matmul(support[:, b, :], xt[:, b * P:(b + 1) * P], w_sb[:, :],
                                           start=True, stop=True)
                ins.then_inc(support_ready, 1)
                pe.wait_ge(row_parts_ready, r + 1)
                if not first:
                    pe.wait_ge(degree_ready, r)
                for b in range(B):
                    ins = nc.tensor.matmul(deg_ps[:, b:b + 1], row_parts[:, b * P:(b + 1) * P],
                                           ones[:, :], start=True, stop=True)
                ins.then_inc(degree_parts_ready, 1)

            def multiply(bank, s_k, chunk):
                for b in range(B):
                    ins = nc.tensor.matmul(prod[:, bank, :], s_k[:, b, :], chunk(b),
                                           start=(b == 0), stop=(b == B - 1))
                ins.then_inc(chunk_multiplied, 1)

            def turn(p):
                pe.wait_ge(chunk_folded, S * (S - 1) + p + 1)
                if p >= 2:
                    pe.wait_ge(y_ready, B * (p - 1))
                for b in range(B):
                    ins = nc.tensor.transpose(turned[:, p % 2, b, :],
                                              stage[:, p % 2, b * P:(b + 1) * P], ident[:, :])
                ins.then_inc(turned_ready, 1)

            def step(k, shape_of, last=False):
                pe.wait_ge(scaled_ready, B * (k + 1))
                n = cached_count(shape_of)
                for pos in range(S):
                    if pos < n:
                        d = pos
                        r = k - d
                        pe.wait_ge(kept_loaded[d], 16 * (r + 1))
                        at = (CACHE_AT[d] + r % (d + 1)) * (B * C)
                        chunk = lambda b: cache[:, bass.ds(at + b * C, C)]
                    else:
                        q = stream_before(shape_of) + pos - n
                        rounds = q // RING + 1 + (k - shape_of) * (stream_count(shape_of) // RING)
                        pe.wait_ge(stream_loaded[q % RING], 16 * rounds)
                        chunk = lambda b: stream[:, q % RING, b, :]
                    if shape_of > 0 or pos >= BANKS:
                        pe.wait_ge(chunk_folded, S * k + pos + 1 - BANKS)
                    multiply(pos % BANKS, scaled[:, shape_of % 2], chunk)
                    if pos == S - 1 - TAIL and not last:
                        prepare(k + 1)
                    if last and pos >= 1:
                        turn(pos - 1)

            prepare(0, first=True)
            for k in range(NEAR):
                step(k, k)
            with pe.Fori(NEAR, S - 1, 2) as k:
                step(k, NEAR)
                step(k + 1, NEAR + 1)
            step(S - 1, S - 1, last=True)
            turn(S - 1)

        @block.vector
        def _(dve):
            added = [0]
            folded = [0]
            waiting = []

            def add_row():
                if not waiting:
                    return
                n, r, last = waiting.pop()
                dve.wait_ge(quad_done, n + 1)
                if added[0]:
                    dve.wait_ge(row_added, added[0])
                if last and r > 0:
                    dve.wait_ge(degree_parts_ready, r)
                ins = nc.vector.tensor_tensor(row_parts[:, :] if last else row_acc[:, r, :],
                                              row_acc[:, r, :], quad_sum[:, n % 2, :], ALU.add)
                ins.then_inc(row_parts_ready if last else row_added, 1)
                if not last:
                    added[0] += 1

            def sum_chunk(n, chunk, r, first, last):
                if n:
                    dve.wait_ge(quad_done, n)
                nc.vector.tensor_tensor(pair_sum[:, :, :], chunk[:, 0:2, :], chunk[:, 2:4, :],
                                        ALU.add).then_inc(pair_done, 1)
                if added[0]:
                    dve.wait_ge(row_added, added[0])
                add_row()
                dve.wait_ge(pair_done, n + 1)
                nc.vector.tensor_tensor(row_acc[:, r, :] if first else quad_sum[:, n % 2, :],
                                        pair_sum[:, 0, :], pair_sum[:, 1, :],
                                        ALU.add).then_inc(quad_done, 1)
                if not first:
                    waiting.append((n, r, last))

            def fold(k, pos):
                i = chunk_of(k, pos)
                dve.wait_ge(chunk_multiplied, S * k + pos + 1)
                acc = out_acc[:, i * C:(i + 1) * C]
                if k == 0:
                    ins = nc.vector.tensor_copy(acc, prod[:, pos % BANKS, :])
                else:
                    dve.wait_ge(chunk_folded, S * k + pos - (S - BANKS) + 1)
                    target = acc
                    if k == S - 1:
                        target = stage[:, pos % 2, :]
                        if pos >= 2:
                            dve.wait_ge(turned_ready, pos - 1)
                    ins = nc.vector.tensor_tensor(target, prod[:, pos % BANKS, :], acc, ALU.add)
                ins.then_inc(chunk_folded, 1)

            def fold_up_to(total):
                while folded[0] < total:
                    fold(folded[0] // S, folded[0] % S)
                    folded[0] += 1

            def sum_far(r):
                dve.wait_ge(natural_summed, B * sum(far_count(t) for t in range(r + 1)))
                nc.vector.tensor_reduce(far_sum[:, :], far_parts[:, :, 0:far_count(r)], AX_X,
                                        ALU.add).then_inc(far_reduced, 1)

            def finish_degree(r):
                dve.wait_ge(degree_parts_ready, r + 1)
                if r > 0:
                    dve.wait_ge(d_is_ready, r)
                if far_count(r):
                    dve.wait_ge(far_reduced, r + 1)
                    ins = nc.vector.tensor_tensor(degree[:, :], deg_ps[:, 0:B], far_sum[:, :],
                                                  ALU.add)
                else:
                    ins = nc.vector.tensor_copy(degree[:, :], deg_ps[:, 0:B])
                ins.then_inc(degree_ready, 1)

            def sum_kept(r, d):
                dve.wait_ge(kept_loaded[d], 16 * (r + 1))
                at = (CACHE_AT[d] + r % (d + 1)) * B * C
                slot = cache[:, at:at + B * C]\
                    .rearrange("p (b c) -> p b c", b=B)
                sum_chunk(summed["kept", r, d], slot, r, r == 0 and d == 0,
                          d == kept_count(r) - 1)

            def sum_stream(k, m):
                q = stream_before(k) + m
                dve.wait_ge(stream_loaded[q % RING], 16 * (q // RING + 1))
                sum_chunk(summed["stream", k, m], stream[:, q % RING, :, :], k + 1 + m, k == 0,
                          False)

            for d in range(kept_count(0)):
                sum_kept(0, d)
            add_row()
            sum_far(0)
            finish_degree(0)

            for k in range(S - 1):
                for kind, m in load_order(k):
                    if kind == "stream":
                        pos = cached_count(k) + m
                        if pos == S - TAIL:
                            add_row()
                            if far_count(k + 1):
                                sum_far(k + 1)
                            fold_up_to(S * k + S - TAIL)
                            finish_degree(k + 1)
                        fold_up_to(S * k + max(0, pos - 1))
                        if ("stream", k, m) in summed:
                            sum_stream(k, m)
                    if kind == "kept":
                        sum_kept(k + 1, m)

            def residual(p):
                i = chunk_of(S - 1, p)
                dve.wait_ge(turned_ready, p + 1)
                dve.wait_ge(xres_loaded[p % XR], 16 * (p // XR + 1))
                if p >= 2:
                    dve.wait_ge(result_ready, B * (p - 1))
                for b in range(B):
                    nc.vector.scalar_tensor_tensor(
                        out=y[:, p % 2, b, :], in0=turned[:, p % 2, b, :],
                        scalar=d_is[:, i, b:b + 1], in1=x_res[:, p % XR, b, :],
                        op0=ALU.mult, op1=ALU.add).then_inc(y_ready, 1)
                for b in range(B):
                    dve.wait_ge(y_ready, B * p + b + 1)
                    nc.vector.bn_stats(stats[:, p % 2, b, :], y[:, p % 2, b, :])\
                        .then_inc(stats_ready, 1)
                for b in range(B):
                    dve.wait_ge(stats_ready, B * p + b + 1)
                    nc.vector.bn_aggr(mean_var[:, p % 2, b, :], stats[:, p % 2, b, :])\
                        .then_inc(mean_ready, 1)
                dve.wait_ge(mean_ready, B * (p + 1))
                nc.vector.tensor_scalar(var_eps[:, p % 2, :], mean_var[:, p % 2, :, 1], EPS, None,
                                        ALU.add).then_inc(var_ready, 1)

            def shift_mean(p):
                dve.wait_ge(rstd_ready, p + 1)
                nc.vector.scalar_tensor_tensor(
                    out=shift[:, p % 2, :], in0=mean_var[:, p % 2, :, 0], scalar=-1.0,
                    in1=rstd[:, p % 2, :], op0=ALU.mult, op1=ALU.mult).then_inc(shift_ready, 1)

            fold_up_to(S * (S - 1))
            for p in range(S):
                fold_up_to(S * (S - 1) + p + 1)
                if p >= 1:
                    residual(p - 1)
                    shift_mean(p - 1)
            residual(S - 1)
            shift_mean(S - 1)


def kernel(x, adj, L0_gnn_weight):
    import numpy as np
    import concourse.bacc as bacc
    from concourse.bass_utils import run_bass_kernel_spmd

    x, adj = np.asarray(x), np.asarray(adj)
    blocks = adj.reshape(S, B, P, S, B, P)
    arrays = {
        "adj_t": np.ascontiguousarray(blocks.transpose(3, 0, 5, 4, 1, 2)).reshape(S, S, P, B, C),
        "adj_n": np.ascontiguousarray(blocks.transpose(0, 3, 1, 2, 4, 5)).reshape(S, S, B, P, C),
        "x_t": np.ascontiguousarray(x.reshape(S, C, F).transpose(0, 2, 1)),
        "x_n": np.ascontiguousarray(x.reshape(S, B, P, F).transpose(0, 2, 1, 3)),
        "weight": np.ascontiguousarray(L0_gnn_weight),
    }
    nc = bacc.Bacc("TRN2", target_bir_lowering=False, num_devices=1)
    aps = {name: nc.dram_tensor(name, a.shape, F32, kind="ExternalInput").ap()
           for name, a in arrays.items()}
    out = nc.dram_tensor("out", (S, P, B, F), F32, kind="ExternalOutput").ap()
    gnn_layernorm(nc, out=out, **aps)
    got = run_bass_kernel_spmd(nc, [arrays], core_ids=[0]).results[0]["out"]
    return np.ascontiguousarray(got.transpose(0, 2, 1, 3)).reshape(N, F)
```

```python
from contextlib import ExitStack

import concourse.bass as bass
from concourse import mybir

F32 = mybir.dt.float32
F32R = mybir.dt.float32r
ALU = mybir.AluOpType
ACT = mybir.ActivationFunctionType
AX_X = mybir.AxisListType.X

P = 128
N = 8192
F = 128
B = 4
C = B * P
S = N // C
NEAR = 3
RING = 4
BANKS = 4
FAR_RING = 6
EPS = 1e-5
LOAD_TIME = 0.85
LOAD_LATENCY = 0.55
SUM_TIME = 0.7
SPLIT_TIME = 0.75
SPLIT_SOONER = 1.5
FOLD_LATER = 0.6
KEPT_FIRST, KEPT_STEP = 1, 3
XR = 8
X_ROW = S - 1 - 2 * NEAR
OLD = 12
TAIL = 2

FIRST_SPLIT = 11
SPLIT_AT = {k: (2, 4, 6, 7, 8, 9, 10, 11, 12, 13)
            for k in range(FIRST_SPLIT, S - 1)}
SPLIT_RING = 2
SPLITS = len(SPLIT_AT[FIRST_SPLIT])

CACHE_AT = [d * (d + 1) // 2 for d in range(NEAR + 1)]
CACHE_SLOTS = CACHE_AT[NEAR] + NEAR + 1


def cached_count(k):
    return 1 + min(NEAR, k)


def stream_count(k):
    return S - cached_count(k)


def stream_before(k):
    return sum(stream_count(t) for t in range(k))


def far_count(r):
    return max(0, S - 1 - NEAR - r)


def kept_count(r):
    return min(NEAR, S - 1 - r) + 1


def is_split(k, pos):
    return k in SPLIT_AT and pos in SPLIT_AT[k]


def split_index(k, pos):
    return B * (SPLITS * (k - FIRST_SPLIT) + SPLIT_AT[k].index(pos))


def split_before(k, pos):
    at = split_index(k, pos) // B - SPLIT_RING
    if at < 0:
        return None
    k = FIRST_SPLIT + at // SPLITS
    return k, SPLIT_AT[k][at % SPLITS]


def split_slot(k, pos):
    return split_index(k, pos) // B % SPLIT_RING


def load_order(k):
    kept = [("kept", d) for d in range(kept_count(k + 1))] if k + 1 < S else []
    far = [("far", n) for n in range(far_count(k + 1))] if k + 1 < S else []
    if k < 0:
        out = []
        while kept or far:
            out += kept[:1] + far[:3]
            kept, far = kept[1:], far[3:]
        return out
    streams = [("stream", m) for m in range(stream_count(k))]
    head = cached_count(k) + 1
    extras = far[:head] + kept + far[head:]
    out, room, extras = streams[:RING] + extras[:head], streams[RING:-TAIL], extras[head:]
    for i, s in enumerate(room):
        out += extras[len(extras) * i // len(room):len(extras) * (i + 1) // len(room)]
        out.append(s)
    return out + streams[-TAIL:]


def vector_order():
    order = []
    loads_end = 0.0
    end = {}
    freed = []
    last_end = 0.0
    scaled_at = 0.0

    def product(k, pos, begin):
        nonlocal last_end
        last_end = max(last_end, begin, scaled_at) + (SPLIT_TIME if is_split(k, pos) else 1)
        end[k, pos] = last_end
        order.append((last_end + FOLD_LATER, "fold", k, pos))
        if is_split(k, pos):
            order.append((last_end - SPLIT_TIME - SPLIT_SOONER, "split", k, pos))

    for k in range(S):
        row_there = last_end
        kept_there = []
        for pos in range(cached_count(k)):
            product(k, pos, last_end)
        for kind, m in load_order(k):
            begin = loads_end
            if kind == "stream" and len(freed) >= RING:
                begin = max(begin, freed[-RING])
            if kind == "kept" and (k, m) in end and k >= m:
                begin = max(begin, end[k, m])
            loads_end = begin + LOAD_TIME
            there = loads_end + LOAD_LATENCY
            if kind == "kept":
                kept_there.append(there)
            if kind == "stream":
                if k + 1 + m < S:
                    order.append((there, "stream", k, m))
                product(k, cached_count(k) + m, there)
                freed.append(last_end)
            else:
                row_there = there
        for d, there in enumerate(kept_there):
            at = max(there, end[k, KEPT_FIRST + KEPT_STEP * d])
            order.append((at, "kept", k + 1, d))
            row_there = max(row_there, at)
        if k + 1 < S:
            at = max(row_there + SUM_TIME, end[k, S - TAIL - 1]) + 0.2
            order.append((at, "degree", k + 1, 0))
            scaled_at = at + 1
    return [work for _, *work in sorted(order, key=lambda work: work[0])]


def gnn_layernorm(nc, adj_t, adj_n, x_t, x_n, weight, out):
    with ExitStack() as ctx:
        def sb(name, shape):
            return ctx.enter_context(nc.sbuf_tensor(name, shape, F32))

        def psum(name, shape):
            return ctx.enter_context(nc.psum_tensor(name, shape, F32))

        def sem(name):
            return ctx.enter_context(nc.semaphore(name))

        stream = sb("stream", [P, RING, B, C])
        cache = sb("cache", [P, CACHE_SLOTS * B * C])
        out_acc = sb("out_acc", [P, N])
        pair_sum = sb("pair_sum", [P, 2, C])
        quad_sum = sb("quad_sum", [P, 2, C])
        row_parts = sb("row_parts", [P, C])
        scaled = sb("scaled", [P, 2, B, F])
        xt = sb("xt", [P, C])
        w_sb = sb("w_sb", [P, F])
        ident = sb("ident", [P, P])
        ones = sb("ones", [P, 1])
        minus_half = sb("minus_half", [P, B])
        far_parts = sb("far_parts", [P, B, S])
        far_sum = sb("far_sum", [P, B])
        degree = sb("degree", [P, B])
        d_is = sb("d_is", [P, S, B])
        stats = sb("stats", [P, 2, B, 6])
        mean_var = sb("mean_var", [P, 2, B, 2])
        var_eps = sb("var_eps", [P, 2, B])
        rstd = sb("rstd", [P, 2, B])
        shift = sb("shift", [P, 2, B])
        row_acc_new = sb("row_acc_new", [P, S - OLD, C])
        with nc.sbuf_tensor("natural", [P, FAR_RING, C], F32) as natural:
            with nc.sbuf_tensor("row_acc_old", [P, OLD, C], F32) as row_acc_old:
                pass
        hi = ctx.enter_context(nc.sbuf_tensor("hi", [P, SPLIT_RING, B, C], F32R))
        lo = ctx.enter_context(nc.sbuf_tensor("lo", [P, SPLIT_RING, B, C], F32R))
        s_hi = ctx.enter_context(nc.sbuf_tensor("s_hi", [P, B, F], F32R))
        s_lo = ctx.enter_context(nc.sbuf_tensor("s_lo", [P, B, F], F32R))

        def row_acc(r):
            return row_acc_old[:, r, :] if r < OLD else row_acc_new[:, r - OLD, :]

        stage = row_acc_new[:, 0:2, :]
        y = row_acc_new[:, 2:4, :].rearrange("p a (b f) -> p a b f", b=B)
        result_at = (CACHE_AT[NEAR] + (X_ROW + 2) % (NEAR + 1)) * B * C
        result = cache[:, result_at:result_at + 2 * B * F]\
            .rearrange("p (a b f) -> p a b f", a=2, b=B)
        x_at = (CACHE_AT[NEAR] + X_ROW % (NEAR + 1)) * B * C
        x_res = cache[:, x_at:x_at + XR * B * F].rearrange("p (a b f) -> p a b f", a=XR, b=B)

        prod = psum("prod", [P, BANKS, C])
        support = psum("support", [P, B, F])
        deg_ps = psum("deg_ps", [P, C])
        turned = psum("turned", [P, 2, B, F])

        stream_loaded = [sem(f"stream_loaded{i}") for i in range(RING)]
        kept_loaded = [sem(f"kept_loaded{i}") for i in range(NEAR + 1)]
        natural_loaded = [sem(f"natural_loaded{i}") for i in range(FAR_RING)]
        weight_loaded = sem("weight_loaded")
        xt_loaded = sem("xt_loaded")
        xres_loaded = [sem(f"xres_loaded{i}") for i in range(XR)]
        consts_ready = sem("consts_ready")
        ident_zero = sem("ident_zero")
        chunk_multiplied = sem("chunk_multiplied")
        chunk_folded = sem("chunk_folded")
        pair_done = sem("pair_done")
        quad_done = sem("quad_done")
        row_added = sem("row_added")
        natural_summed = sem("natural_summed")
        far_reduced = sem("far_reduced")
        row_parts_ready = sem("row_parts_ready")
        hi_ready = sem("hi_ready")
        lo_ready = sem("lo_ready")
        split_multiplied = sem("split_multiplied")
        s_hi_ready = sem("s_hi_ready")
        s_lo_ready = sem("s_lo_ready")
        support_ready = sem("support_ready")
        degree_parts_ready = sem("degree_parts_ready")
        degree_ready = sem("degree_ready")
        d_is_ready = sem("d_is_ready")
        scaled_ready = sem("scaled_ready")
        turned_ready = sem("turned_ready")
        y_ready = sem("y_ready")
        stats_ready = sem("stats_ready")
        mean_ready = sem("mean_ready")
        var_ready = sem("var_ready")
        rstd_ready = sem("rstd_ready")
        shift_ready = sem("shift_ready")
        result_ready = sem("result_ready")
        stored = [sem(f"stored{i}") for i in range(2)]

        def chunk_of(k, pos):
            n = cached_count(k)
            return k - pos if pos < n else (k + 1 + pos - n) % S

        def chunk_in(k, pos):
            if pos < cached_count(k):
                r = k - pos
                at = (CACHE_AT[pos] + r % (pos + 1)) * B * C
                return (cache[:, at:at + B * C].rearrange("p (b c) -> p b c", b=B),
                        kept_loaded[pos], 16 * (r + 1))
            q = stream_before(k) + pos - cached_count(k)
            return stream[:, q % RING, :, :], stream_loaded[q % RING], 16 * (q // RING + 1)

        def wait_split_used(engine, k, pos, b):
            before = split_before(k, pos)
            if before is None:
                return
            if b == B - 1:
                engine.wait_ge(chunk_multiplied, S * before[0] + before[1] + 1)
            else:
                engine.wait_ge(split_multiplied, split_index(*before) // B * (B - 1) + b + 1)

        order = vector_order()
        sums = [("kept", 0, d) for d in range(kept_count(0))]
        sums += [tuple(work) for work in order if work[0] in ("kept", "stream")]
        summed = {work: n for n, work in enumerate(sums)}

        block = ctx.enter_context(nc.Block())

        @block.sync
        def _(sp):
            sp.dma_start(w_sb[:, :], weight).then_inc(weight_loaded, 16)

            def load_xt(r):
                if r > 0:
                    sp.wait_ge(support_ready, r)
                sp.dma_start(xt[:, :], x_t[r]).then_inc(xt_loaded, 16)

            def load_x_res(p):
                if p >= XR:
                    sp.wait_ge(y_ready, B * (p - XR + 1))
                sp.dma_start(x_res[:, p % XR, :, :], x_n[chunk_of(S - 1, p)])\
                    .then_inc(xres_loaded[p % XR], 16)

            far_seen = 0
            load_xt(0)
            for k in range(-1, S):
                if k >= 0 and k + 1 < S:
                    load_xt(k + 1)
                if k == S - 2:
                    sp.wait_ge(chunk_multiplied, S * (X_ROW + 1 + NEAR) + NEAR + 1)
                    for p in range(XR):
                        load_x_res(p)
                for kind, m in load_order(k):
                    if kind == "stream":
                        q = stream_before(k) + m
                        if q >= RING:
                            kk, mm = k, m - RING
                            while mm < 0:
                                kk -= 1
                                mm += stream_count(kk)
                            sp.wait_ge(chunk_multiplied, S * kk + cached_count(kk) + mm + 1)
                            if ("stream", kk, mm) in summed:
                                sp.wait_ge(pair_done, summed["stream", kk, mm] + 1)
                        sp.dma_start(stream[:, q % RING, :, :], adj_t[k, (k + 1 + m) % S])\
                            .then_inc(stream_loaded[q % RING], 16)
                        if k == S - 1 and m >= 3 and XR + m - 3 < S:
                            load_x_res(XR + m - 3)
                    if kind == "kept":
                        r, d = k + 1, m
                        if r - d - 1 >= 0:
                            sp.wait_ge(chunk_multiplied, S * k + d + 1)
                        if r > 0:
                            sp.wait_ge(kept_loaded[d], 16 * r)
                        at = (CACHE_AT[d] + r % (d + 1)) * B * C
                        sp.dma_start(cache[:, at:at + B * C],
                                     adj_t[r + d, r].rearrange("p b c -> p (b c)"))\
                            .then_inc(kept_loaded[d], 16)
                    if kind == "far":
                        r, n = k + 1, m
                        for b in range(B):
                            z = B * far_seen + b
                            if z >= FAR_RING:
                                sp.wait_ge(natural_summed, z - FAR_RING + 1)
                            sp.dma_start(natural[:, z % FAR_RING, :],
                                         adj_n[r, r + NEAR + 1 + n, b])\
                                .then_inc(natural_loaded[z % FAR_RING], 16)
                        far_seen += 1

        @block.gpsimd
        def _(pool):
            nc.gpsimd.memset(ident[:, :], 0.0).then_inc(ident_zero, 1)
            nc.gpsimd.memset(ones[:, :], 1.0).then_inc(consts_ready, 1)
            nc.gpsimd.memset(minus_half[:, :], -0.5).then_inc(consts_ready, 1)
            pool.wait_ge(ident_zero, 1)
            nc.gpsimd.affine_select(out=ident[:, :], in_=ident[:, :], compare_op=ALU.not_equal,
                                    fill=1.0, base=0, pattern=[[-1, P]], channel_multiplier=1)\
                .then_inc(consts_ready, 1)
            pool.wait_ge(consts_ready, 3)
            for r in range(S):
                pool.wait_ge(degree_ready, r + 1)
                nc.gpsimd.tensor_tensor(d_is[:, r, :], degree[:, :], minus_half[:, :], ALU.pow)\
                    .then_inc(d_is_ready, 1)
            for p in range(S):
                pool.wait_ge(var_ready, p + 1)
                if p >= 2:
                    pool.wait_ge(result_ready, B * (p - 1))
                nc.gpsimd.tensor_tensor(rstd[:, p % 2, :], var_eps[:, p % 2, :], minus_half[:, :],
                                        ALU.pow).then_inc(rstd_ready, 1)

        @block.scalar
        def _(act):
            far_seen = [0]

            def sum_far_chunk(r, n):
                if n == 0 and r > 0:
                    act.wait_ge(far_reduced, r)
                for b in range(B):
                    z = B * far_seen[0] + b
                    act.wait_ge(natural_loaded[z % FAR_RING], 16 * (z // FAR_RING + 1))
                    block_in = natural[:, z % FAR_RING, :]
                    nc.scalar.activation(block_in, block_in, ACT.Copy,
                                         accum_out=far_parts[:, b, n:n + 1])\
                        .then_inc(natural_summed, 1)
                far_seen[0] += 1

            def scale_support(r):
                act.wait_ge(support_ready, r + 1)
                act.wait_ge(d_is_ready, r + 1)
                if r >= 2:
                    act.wait_ge(chunk_multiplied, S * (r - 1))
                for b in range(B):
                    nc.scalar.activation(scaled[:, r % 2, b, :], support[:, b, :], ACT.Copy,
                                         scale=d_is[:, r, b:b + 1]).then_inc(scaled_ready, 1)
                if r not in SPLIT_AT:
                    return
                if r > FIRST_SPLIT:
                    act.wait_ge(chunk_multiplied, S * (r - 1) + SPLIT_AT[r - 1][-1] + 1)
                else:
                    act.wait_ge(row_parts_ready, OLD)
                    act.wait_ge(natural_summed, B * sum(far_count(t) for t in range(S)))
                act.wait_ge(scaled_ready, B * (r + 1))
                nc.scalar.activation(s_hi[:, :, :], scaled[:, r % 2, :, :], ACT.Copy)\
                    .then_inc(s_hi_ready, 1)

            def split_high(k, pos):
                if not is_split(k, pos):
                    return
                chunk, loaded, count = chunk_in(k, pos)
                act.wait_ge(loaded, count)
                for b in range(B):
                    z = split_index(k, pos) + b
                    wait_split_used(act, k, pos, b)
                    nc.scalar.activation(hi[:, split_slot(k, pos), b, :], chunk[:, b, :],
                                         ACT.Copy)\
                        .then_inc(hi_ready, 1)

            def normalise(p):
                act.wait_ge(shift_ready, p + 1)
                if p >= 2:
                    act.wait_ge(stored[p % 2], 16 * (p // 2))
                for b in range(B):
                    nc.scalar.activation(result[:, p % 2, b, :], y[:, p % 2, b, :], ACT.Identity,
                                         scale=rstd[:, p % 2, b:b + 1],
                                         bias=shift[:, p % 2, b:b + 1]).then_inc(result_ready, 1)
                act.wait_ge(result_ready, B * (p + 1))
                act.dma_start(out[chunk_of(S - 1, p)], result[:, p % 2, :, :])\
                    .then_inc(stored[p % 2], 16)

            for k in range(-1, S - 1):
                if k >= 0:
                    for pos in range(cached_count(k)):
                        split_high(k, pos)
                for kind, m in load_order(k):
                    if kind == "far":
                        sum_far_chunk(k + 1, m)
                    if kind == "stream":
                        pos = cached_count(k) + m
                        if pos == S - TAIL:
                            scale_support(k + 1)
                        split_high(k, pos)
                if k < 0:
                    scale_support(0)
            for p in range(S):
                normalise(p)
            for i in range(2):
                act.wait_ge(stored[i], 16 * (S // 2))

        @block.tensor
        def _(pe):
            def prepare(r, first=False):
                pe.wait_ge(xt_loaded, 16 * (r + 1))
                if first:
                    pe.wait_ge(weight_loaded, 16)
                    pe.wait_ge(consts_ready, 3)
                else:
                    pe.wait_ge(scaled_ready, B * r)
                for b in range(B):
                    ins = nc.tensor.matmul(support[:, b, :], xt[:, b * P:(b + 1) * P], w_sb[:, :],
                                           start=True, stop=True)
                ins.then_inc(support_ready, 1)
                pe.wait_ge(row_parts_ready, r + 1)
                if not first:
                    pe.wait_ge(degree_ready, r)
                for b in range(B):
                    ins = nc.tensor.matmul(deg_ps[:, b:b + 1], row_parts[:, b * P:(b + 1) * P],
                                           ones[:, :], start=True, stop=True)
                ins.then_inc(degree_parts_ready, 1)

            def multiply(bank, s_k, chunk, turned_between=None):
                for b in range(B):
                    if turned_between is not None and b == B // 2:
                        turn(turned_between)
                    ins = nc.tensor.matmul(prod[:, bank, :], s_k[:, b, :], chunk(b),
                                           start=(b == 0), stop=(b == B - 1))
                ins.then_inc(chunk_multiplied, 1)

            def multiply_split(bank, slot, index):
                for b in range(B):
                    pe.wait_ge(lo_ready, index + b + 1)
                    nc.tensor.matmul(prod[:, bank, :], s_hi[:, b, :], hi[:, slot, b, :],
                                     start=(b == 0), stop=False)
                    nc.tensor.matmul(prod[:, bank, :], s_lo[:, b, :], hi[:, slot, b, :],
                                     start=False, stop=False)
                    ins = nc.tensor.matmul(prod[:, bank, :], s_hi[:, b, :], lo[:, slot, b, :],
                                           start=False, stop=(b == B - 1))
                    ins.then_inc(split_multiplied if b < B - 1 else chunk_multiplied, 1)

            def turn(p):
                pe.wait_ge(chunk_folded, S * (S - 1) + p + 1)
                if p >= 2:
                    pe.wait_ge(y_ready, B * (p - 1))
                for b in range(B):
                    ins = nc.tensor.transpose(turned[:, p % 2, b, :],
                                              stage[:, p % 2, b * P:(b + 1) * P], ident[:, :])
                ins.then_inc(turned_ready, 1)

            def step(k, shape_of, last=False):
                pe.wait_ge(scaled_ready, B * (k + 1))
                n = cached_count(shape_of)
                for pos in range(S):
                    if is_split(shape_of, pos):
                        if pos == SPLIT_AT[shape_of][0]:
                            pe.wait_ge(s_lo_ready, k - FIRST_SPLIT + 1)
                    elif pos < n:
                        d = pos
                        r = k - d
                        pe.wait_ge(kept_loaded[d], 16 * (r + 1))
                        at = (CACHE_AT[d] + r % (d + 1)) * (B * C)
                        chunk = lambda b: cache[:, bass.ds(at + b * C, C)]
                    else:
                        q = stream_before(shape_of) + pos - n
                        rounds = q // RING + 1 + (k - shape_of) * (stream_count(shape_of) // RING)
                        pe.wait_ge(stream_loaded[q % RING], 16 * rounds)
                        chunk = lambda b: stream[:, q % RING, b, :]
                    if shape_of > 0 or pos >= BANKS:
                        pe.wait_ge(chunk_folded, S * k + pos + 1 - BANKS)
                    if is_split(shape_of, pos):
                        index = split_index(shape_of, pos) + B * SPLITS * (k - shape_of)
                        multiply_split(pos % BANKS, split_slot(shape_of, pos), index)
                    else:
                        multiply(pos % BANKS, scaled[:, shape_of % 2], chunk,
                                 pos - 1 if last and pos >= 1 else None)
                    if pos == S - 1 - TAIL and not last:
                        prepare(k + 1)

            prepare(0, first=True)
            for k in range(NEAR):
                step(k, k)
            with pe.Fori(NEAR, FIRST_SPLIT, 2) as k:
                step(k, NEAR)
                step(k + 1, NEAR + 1)
            with pe.Fori(FIRST_SPLIT, S - 1, 2) as k:
                step(k, FIRST_SPLIT)
                step(k + 1, FIRST_SPLIT + 1)
            step(S - 1, S - 1, last=True)
            turn(S - 1)

        @block.vector
        def _(dve):
            added = [0]
            waiting = []

            def add_row():
                if not waiting:
                    return
                n, r, last = waiting.pop()
                dve.wait_ge(quad_done, n + 1)
                if added[0]:
                    dve.wait_ge(row_added, added[0])
                if last and r > 0:
                    dve.wait_ge(degree_parts_ready, r)
                ins = nc.vector.tensor_tensor(row_parts[:, :] if last else row_acc(r),
                                              row_acc(r), quad_sum[:, n % 2, :], ALU.add)
                ins.then_inc(row_parts_ready if last else row_added, 1)
                if not last:
                    added[0] += 1

            def sum_chunk(n, chunk, r, first, last):
                if n:
                    dve.wait_ge(quad_done, n)
                nc.vector.tensor_tensor(pair_sum[:, :, :], chunk[:, 0:2, :], chunk[:, 2:4, :],
                                        ALU.add).then_inc(pair_done, 1)
                if added[0]:
                    dve.wait_ge(row_added, added[0])
                add_row()
                dve.wait_ge(pair_done, n + 1)
                nc.vector.tensor_tensor(row_acc(r) if first else quad_sum[:, n % 2, :],
                                        pair_sum[:, 0, :], pair_sum[:, 1, :],
                                        ALU.add).then_inc(quad_done, 1)
                if not first:
                    waiting.append((n, r, last))
                if last:
                    add_row()

            def fold(k, pos):
                i = chunk_of(k, pos)
                dve.wait_ge(chunk_multiplied, S * k + pos + 1)
                acc = out_acc[:, i * C:(i + 1) * C]
                if k == 0:
                    ins = nc.vector.tensor_copy(acc, prod[:, pos % BANKS, :])
                else:
                    dve.wait_ge(chunk_folded, S * k + pos - (S - BANKS) + 1)
                    target = acc
                    if k == S - 1:
                        target = stage[:, pos % 2, :]
                        if pos >= 2:
                            dve.wait_ge(turned_ready, pos - 1)
                    ins = nc.vector.tensor_tensor(target, prod[:, pos % BANKS, :], acc, ALU.add)
                ins.then_inc(chunk_folded, 1)

            def split_low(k, pos):
                if pos == SPLIT_AT[k][0]:
                    dve.wait_ge(s_hi_ready, k - FIRST_SPLIT + 1)
                    if k > FIRST_SPLIT:
                        dve.wait_ge(chunk_multiplied, S * (k - 1) + SPLIT_AT[k - 1][-1] + 1)
                    nc.vector.tensor_tensor(s_lo[:, :, :], scaled[:, k % 2, :, :],
                                            s_hi[:, :, :].bitcast(F32), ALU.subtract)\
                        .then_inc(s_lo_ready, 1)
                chunk, loaded, count = chunk_in(k, pos)
                dve.wait_ge(loaded, count)
                for b in range(B):
                    z = split_index(k, pos) + b
                    dve.wait_ge(hi_ready, z + 1)
                    wait_split_used(dve, k, pos, b)
                    slot = split_slot(k, pos)
                    nc.vector.tensor_tensor(lo[:, slot, b, :], chunk[:, b, :],
                                            hi[:, slot, b, :].bitcast(F32), ALU.subtract)\
                        .then_inc(lo_ready, 1)

            def sum_far(r):
                dve.wait_ge(natural_summed, B * sum(far_count(t) for t in range(r + 1)))
                nc.vector.tensor_reduce(far_sum[:, :], far_parts[:, :, 0:far_count(r)], AX_X,
                                        ALU.add).then_inc(far_reduced, 1)

            def finish_degree(r):
                dve.wait_ge(degree_parts_ready, r + 1)
                if r > 0:
                    dve.wait_ge(d_is_ready, r)
                if far_count(r):
                    dve.wait_ge(far_reduced, r + 1)
                    ins = nc.vector.tensor_tensor(degree[:, :], deg_ps[:, 0:B], far_sum[:, :],
                                                  ALU.add)
                else:
                    ins = nc.vector.tensor_copy(degree[:, :], deg_ps[:, 0:B])
                ins.then_inc(degree_ready, 1)

            def sum_kept(r, d):
                dve.wait_ge(kept_loaded[d], 16 * (r + 1))
                at = (CACHE_AT[d] + r % (d + 1)) * B * C
                slot = cache[:, at:at + B * C]\
                    .rearrange("p (b c) -> p b c", b=B)
                sum_chunk(summed["kept", r, d], slot, r, r == 0 and d == 0,
                          d == kept_count(r) - 1)

            def sum_stream(k, m):
                q = stream_before(k) + m
                dve.wait_ge(stream_loaded[q % RING], 16 * (q // RING + 1))
                sum_chunk(summed["stream", k, m], stream[:, q % RING, :, :], k + 1 + m, k == 0,
                          False)

            for d in range(kept_count(0)):
                sum_kept(0, d)
            sum_far(0)
            finish_degree(0)

            last_step = order.index(["fold", S - 1, 0])
            for what, a, b in order[:last_step]:
                if what == "kept":
                    sum_kept(a, b)
                if what == "stream":
                    sum_stream(a, b)
                if what == "fold":
                    fold(a, b)
                if what == "split":
                    split_low(a, b)
                if what == "degree":
                    if far_count(a):
                        sum_far(a)
                    finish_degree(a)

            def residual(p):
                i = chunk_of(S - 1, p)
                dve.wait_ge(turned_ready, p + 1)
                dve.wait_ge(xres_loaded[p % XR], 16 * (p // XR + 1))
                if p >= 2:
                    dve.wait_ge(result_ready, B * (p - 1))
                for b in range(B):
                    nc.vector.scalar_tensor_tensor(
                        out=y[:, p % 2, b, :], in0=turned[:, p % 2, b, :],
                        scalar=d_is[:, i, b:b + 1], in1=x_res[:, p % XR, b, :],
                        op0=ALU.mult, op1=ALU.add).then_inc(y_ready, 1)
                for b in range(B):
                    dve.wait_ge(y_ready, B * p + b + 1)
                    nc.vector.bn_stats(stats[:, p % 2, b, :], y[:, p % 2, b, :])\
                        .then_inc(stats_ready, 1)
                for b in range(B):
                    dve.wait_ge(stats_ready, B * p + b + 1)
                    nc.vector.bn_aggr(mean_var[:, p % 2, b, :], stats[:, p % 2, b, :])\
                        .then_inc(mean_ready, 1)
                dve.wait_ge(mean_ready, B * (p + 1))
                nc.vector.tensor_scalar(var_eps[:, p % 2, :], mean_var[:, p % 2, :, 1], EPS, None,
                                        ALU.add).then_inc(var_ready, 1)

            def shift_mean(p):
                dve.wait_ge(rstd_ready, p + 1)
                nc.vector.scalar_tensor_tensor(
                    out=shift[:, p % 2, :], in0=mean_var[:, p % 2, :, 0], scalar=-1.0,
                    in1=rstd[:, p % 2, :], op0=ALU.mult, op1=ALU.mult).then_inc(shift_ready, 1)

            for p in range(S):
                if p >= 1:
                    residual(p - 1)
                fold(S - 1, p)
                if p >= 1:
                    shift_mean(p - 1)
            residual(S - 1)
            shift_mean(S - 1)


def kernel(x, adj, L0_gnn_weight):
    import numpy as np
    import concourse.bacc as bacc
    from concourse.bass_utils import run_bass_kernel_spmd

    x, adj = np.asarray(x), np.asarray(adj)
    blocks = adj.reshape(S, B, P, S, B, P)
    arrays = {
        "adj_t": np.ascontiguousarray(blocks.transpose(3, 0, 5, 4, 1, 2)).reshape(S, S, P, B, C),
        "adj_n": np.ascontiguousarray(blocks.transpose(0, 3, 1, 2, 4, 5)).reshape(S, S, B, P, C),
        "x_t": np.ascontiguousarray(x.reshape(S, C, F).transpose(0, 2, 1)),
        "x_n": np.ascontiguousarray(x.reshape(S, B, P, F).transpose(0, 2, 1, 3)),
        "weight": np.ascontiguousarray(L0_gnn_weight),
    }
    nc = bacc.Bacc("TRN2", target_bir_lowering=False, num_devices=1)
    aps = {name: nc.dram_tensor(name, a.shape, F32, kind="ExternalInput").ap()
           for name, a in arrays.items()}
    out = nc.dram_tensor("out", (S, P, B, F), F32, kind="ExternalOutput").ap()
    gnn_layernorm(nc, out=out, **aps)
    got = run_bass_kernel_spmd(nc, [arrays], core_ids=[0]).results[0]["out"]
    return np.ascontiguousarray(got.transpose(0, 2, 1, 3)).reshape(N, F)
```
